# Optimizing a Trainium2 kernel written in Bass

```python
import numpy as np
import jax
import jax.numpy as jnp

def _softmax(x, axis=-1):
    return jax.nn.softmax(x, axis=axis)

def _gelu(x):
    return jax.nn.gelu(x, approximate=True)

def _silu(x):
    return jax.nn.silu(x)

def _sigmoid(x):
    return jax.nn.sigmoid(x)

def _layernorm(x, axis=-1, eps=1e-05):
    m = jnp.mean(x, axis=axis, keepdims=True)
    v = jnp.var(x, axis=axis, keepdims=True)
    return (x - m) / jnp.sqrt(v + eps)

def _scatter_add(tgt, idx, src, axis=0):
    return tgt.at[idx].add(src)

def _segment_sum(src, seg, n):
    return jax.ops.segment_sum(src, seg, n)
kernel_name = 'mk_rec_standalone_d1_rec_r8_c2b940'

def setup_inputs(seed: int=0):
    np.random.seed(seed)
    _w = jnp.asarray

    def _rec_inputs():
        import jax
        import jax.numpy as jnp
        _rk = jax.random.key(seed)
        r_x = jax.random.randint(jax.random.fold_in(_rk, 1), (1024, 20000), 0, 2, jnp.int32)
        return r_x
    r_x = _rec_inputs()

    def _L0_rec_setup():
        import jax, jax.numpy as jnp
        import numpy as np
        B, F, D = (1024, 20000, 16)
        key = jax.random.key(seed)
        k1, k2, k3 = jax.random.split(key, 3)
        x = jax.random.randint(k1, (B, F), 0, 2, dtype=jnp.int32)
        emb_w = jax.random.normal(k2, (F, D), dtype=jnp.float32) * 0.05
        bias_w = jax.random.normal(k3, (F, 1), dtype=jnp.float32) * 0.05
        g_bias = jnp.zeros((), dtype=jnp.float32)
        return {'x': x, 'emb_w': emb_w, 'bias_w': bias_w, 'g_bias': g_bias}
    _L0_rec_all = _L0_rec_setup()
    _L0_rec_in = {k: v for k, v in _L0_rec_all.items() if k in ('emb_w', 'bias_w', 'g_bias')}
    del _L0_rec_all
    return {'r_x': r_x, 'L0_rec_emb_w': _L0_rec_in['emb_w'], 'L0_rec_bias_w': _L0_rec_in['bias_w'], 'L0_rec_g_bias': _L0_rec_in['g_bias']}

def reference(r_x, L0_rec_emb_w, L0_rec_bias_w, L0_rec_g_bias):
    import jax
    import jax.numpy as jnp

    def _L0_rec_ref(x, emb_w, bias_w, g_bias):
        import jax, jax.numpy as jnp
        import numpy as np
        B, F, D = (1024, 20000, 16)
        mask = (x > 0).astype(emb_w.dtype)
        ev = mask @ emb_w
        rowsq = jnp.sum(emb_w * emb_w, axis=1)
        sum_sq = mask @ rowsq
        second = 0.5 * (jnp.sum(ev * ev, axis=-1) - sum_sq)
        linear = g_bias + mask @ bias_w
        return linear + second[:, None]
    y = _L0_rec_ref(r_x, L0_rec_emb_w, L0_rec_bias_w, L0_rec_g_bias)
    return y

_drawn_inputs = setup_inputs


def setup_inputs(seed=0):
    import zlib

    import numpy as np

    out = dict(_drawn_inputs(seed))
    spreads = {}
    factors = {}
    for name, (base, spread) in spreads.items():
        noise = np.random.default_rng([zlib.crc32(name.encode()), seed]).standard_normal(out[name].shape)
        drawn = base * np.exp(spread * noise) if base else spread * noise
        out[name] = jnp.asarray(drawn.astype(out[name].dtype))
    for name, factor in factors.items():
        out[name] = (out[name] * factor).astype(out[name].dtype)
    return out
```

```python
from contextlib import ExitStack

import concourse.bass as bass
from concourse import mybir

BATCH, FEATURES, DIM = 1024, 20000, 16
P = 128
TILES = FEATURES // P
REST = FEATURES - TILES * P
GROUPS = BATCH // P
COLS = DIM + 1
PARTS = 3

X_SLOTS = 6
MASK_SLOTS = 3
PIECE = 4
ROUNDS = 6
TAIL = [4, 4, 2, 1, 1]


def fm_kernel(nc, x_t, emb, bias, g, out):
    fp32, bf16, i32 = mybir.dt.float32, mybir.dt.bfloat16, mybir.dt.int32
    ALU = mybir.AluOpType
    AX_X = mybir.AxisListType.X

    assert ROUNDS * X_SLOTS * PIECE + sum(TAIL) == TILES and len(TAIL) <= X_SLOTS
    assert X_SLOTS % MASK_SLOTS == 0
    USES = X_SLOTS // MASK_SLOTS

    x_main = x_t[0:TILES * P, :].rearrange("(p t) b -> p t b", t=TILES)
    x_rest = x_t[TILES * P:FEATURES, :]
    emb_main = emb[0:TILES * P, :].rearrange("(p t) d -> p t d", t=TILES)
    emb_rest = emb[TILES * P:FEATURES, :]
    bias_main = bias[0:TILES * P, :].rearrange("(p t) o -> p (t o)", t=TILES)
    bias_rest = bias[TILES * P:FEATURES, :]

    ctx = ExitStack()
    with ctx:
        def sb(name, shape, dt):
            return ctx.enter_context(nc.sbuf_tensor(name, shape, dt))

        def sem(name):
            return ctx.enter_context(nc.semaphore(name))

        x_ring = [sb(f"x_ring{s}", [P, PIECE, BATCH], i32) for s in range(X_SLOTS)]
        masks = [sb(f"masks{m}", [P, PIECE, BATCH], bf16) for m in range(MASK_SLOTS)]
        x_rem = sb("x_rem", [REST, BATCH], i32)
        mask_rem = sb("mask_rem", [REST + 1, BATCH], bf16)
        emb_raw = sb("emb_raw", [P, TILES + 1, DIM], fp32)
        emb_left = sb("emb_left", [P, TILES + 1, DIM], fp32)
        lin_raw = sb("lin_raw", [P, TILES + 1], fp32)
        half_sq = sb("half_sq", [P, TILES + 1], fp32)
        lin = sb("lin", [P, TILES + 1], fp32)
        lin_left = sb("lin_left", [P, TILES + 1], fp32)
        weights = sb("weights", [P, TILES + 1, PARTS, COLS], bf16)
        sums = sb("sums", [P, GROUPS, COLS], fp32)
        y = sb("y", [P, GROUPS], fp32)
        acc = ctx.enter_context(nc.psum_tensor("acc", [P, GROUPS, 512], fp32))

        s_blank = sem("s_blank")
        s_ones = sem("s_ones")
        s_w = sem("s_w")
        s_xrem = sem("s_xrem")
        s_prep = sem("s_prep")
        s_maskrem = sem("s_maskrem")
        s_x = [sem(f"s_x{s}") for s in range(X_SLOTS)]
        s_mask = [sem(f"s_mask{s}") for s in range(X_SLOTS)]
        s_used = [sem(f"s_used{m}") for m in range(MASK_SLOTS)]
        s_acc = sem("s_acc")
        s_fin = sem("s_fin")
        s_y = sem("s_y")
        s_out = sem("s_out")
        W_LOADS = 5

        block = ctx.enter_context(nc.Block())

        @block.sync
        def _(sp):
            sp.dma_start(emb_raw[:, 0:TILES, :], emb_main).then_inc(s_w, 16)
            sp.dma_start(lin_raw[:, 0:TILES], bias_main).then_inc(s_w, 16)
            sp.dma_start(x_rem[:, :], x_rest).then_inc(s_xrem, 16)
            for s in range(X_SLOTS):
                sp.dma_start(x_ring[s][:, :, :], x_main[:, s * PIECE:(s + 1) * PIECE, :]).then_inc(s_x[s], 16)
            with sp.Fori(1, ROUNDS) as r:
                for s in range(X_SLOTS):
                    sp.wait_ge(s_mask[s], r)
                    sp.dma_start(x_ring[s][:, :, :],
                                 x_main[:, bass.ds((r * X_SLOTS + s) * PIECE, PIECE), :]).then_inc(s_x[s], 16)
            t = ROUNDS * X_SLOTS * PIECE
            for s, n in enumerate(TAIL):
                sp.wait_ge(s_mask[s], ROUNDS)
                sp.dma_start(x_ring[s][:, 0:n, :], x_main[:, t:t + n, :]).then_inc(s_x[s], 16)
                t += n
            sp.wait_ge(s_y, 1)
            sp.dma_start(out, y[:, :]).then_inc(s_out, 16)
            sp.wait_ge(s_out, 16)

        @block.scalar
        def _(act):
            act.wait_ge(s_blank, 2)
            act.dma_start(emb_raw[0:REST, TILES, :], emb_rest).then_inc(s_w, 16)
            act.dma_start(lin_raw[0:REST, TILES:TILES + 1], bias_rest).then_inc(s_w, 16)
            act.dma_start(lin_raw[REST:REST + 1, TILES:TILES + 1], g).then_inc(s_w, 16)

        @block.gpsimd
        def _(pool):
            nc.gpsimd.memset(emb_raw[:, TILES, :], 0.0).then_inc(s_blank, 1)
            nc.gpsimd.memset(lin_raw[:, TILES:TILES + 1], 0.0).then_inc(s_blank, 1)
            pool.wait_ge(s_blank, 2)
            nc.gpsimd.memset(mask_rem[REST:REST + 1, :], 1.0).then_inc(s_ones, 1)

        @block.vector
        def _(dve):
            steps = [0]

            def done(ins):
                steps[0] += 1
                ins.then_inc(s_prep, 1)
                dve.wait_ge(s_prep, steps[0])

            dve.wait_ge(s_w, 16 * W_LOADS)
            done(nc.vector.tensor_tensor(emb_left[:, :, :], emb_raw[:, :, :], emb_raw[:, :, :], ALU.mult))
            done(nc.vector.tensor_reduce(half_sq[:, :], emb_left[:, :, :], AX_X, ALU.add))
            done(nc.vector.scalar_tensor_tensor(lin[:, :], half_sq[:, :], -0.5, lin_raw[:, :], ALU.mult, ALU.add))

            for whole, left, c0, c1 in ((emb_raw[:, :, :], emb_left[:, :, :], 0, DIM),
                                        (lin[:, :].unsqueeze(2), lin_left[:, :].unsqueeze(2), DIM, COLS)):
                high, mid, low = (weights[:, :, part, c0:c1] for part in range(PARTS))
                done(nc.vector.tensor_copy(high, whole))
                done(nc.vector.tensor_tensor(left, whole, high, ALU.subtract))
                done(nc.vector.tensor_copy(mid, left))
                done(nc.vector.tensor_tensor(low, left, mid, ALU.subtract))

            dve.wait_ge(s_xrem, 16)
            nc.vector.tensor_scalar(mask_rem[0:REST, :], x_rem[:, :], 0.0, None, ALU.is_gt).then_inc(s_maskrem, 1)
            for s in range(X_SLOTS):
                m = s % MASK_SLOTS
                dve.wait_ge(s_x[s], 16)
                if s >= MASK_SLOTS:
                    dve.wait_ge(s_used[m], s // MASK_SLOTS)
                nc.vector.tensor_scalar(masks[m][:, :, :], x_ring[s][:, :, :], 0.0, None,
                                        ALU.is_gt).then_inc(s_mask[s], 1)
            with dve.Fori(1, ROUNDS) as r:
                for s in range(X_SLOTS):
                    m = s % MASK_SLOTS
                    dve.wait_ge(s_x[s], (r + 1) * 16)
                    dve.wait_ge(s_used[m], r * USES + s // MASK_SLOTS)
                    nc.vector.tensor_scalar(masks[m][:, :, :], x_ring[s][:, :, :], 0.0, None,
                                            ALU.is_gt).then_inc(s_mask[s], 1)
            for s, n in enumerate(TAIL):
                m = s % MASK_SLOTS
                dve.wait_ge(s_x[s], (ROUNDS + 1) * 16)
                dve.wait_ge(s_used[m], ROUNDS * USES + s // MASK_SLOTS)
                nc.vector.tensor_scalar(masks[m][:, 0:n, :], x_ring[s][:, 0:n, :], 0.0, None,
                                        ALU.is_gt).then_inc(s_mask[s], 1)

            dve.wait_ge(s_acc, 1)
            parts = acc[:, :, 0:PARTS * COLS].rearrange("p j (k c) -> p j c k", c=COLS)
            nc.vector.tensor_reduce(sums[:, :, :], parts, AX_X, ALU.add).then_inc(s_fin, 1)
            dve.wait_ge(s_fin, 1)
            ev = sums[:, :, 0:DIM]
            nc.vector.scalar_tensor_tensor(ev, ev, 0.5, ev, ALU.mult, ALU.mult).then_inc(s_fin, 1)
            dve.wait_ge(s_fin, 2)
            nc.vector.tensor_reduce(y[:, :], sums[:, :, :], AX_X, ALU.add).then_inc(s_y, 1)

        @block.tensor
        def _(pe):
            PREP_STEPS = 11

            def products(mask, w, start=False, stop=False):
                for j in range(GROUPS):
                    last = nc.tensor.matmul(acc[:, j, 0:PARTS * COLS], mask[:, j * P:(j + 1) * P], w,
                                            start=start, stop=stop)
                return last

            pe.wait_ge(s_prep, PREP_STEPS)
            pe.wait_ge(s_maskrem, 1)
            pe.wait_ge(s_ones, 1)
            products(mask_rem[:, :], weights[0:REST + 1, TILES, :, :].rearrange("p k c -> p (k c)"), start=True)
            with pe.Fori(0, ROUNDS) as r:
                for s in range(X_SLOTS):
                    m = s % MASK_SLOTS
                    pe.wait_ge(s_mask[s], r + 1)
                    for i in range(PIECE):
                        t = (r * X_SLOTS + s) * PIECE + i
                        w = weights[:, bass.ds(t, 1), :, :].rearrange("p t k c -> p (t k c)")
                        last = products(masks[m][:, i, :], w)
                    last.then_inc(s_used[m], 1)
            t = ROUNDS * X_SLOTS * PIECE
            for s, n in enumerate(TAIL):
                m = s % MASK_SLOTS
                pe.wait_ge(s_mask[s], ROUNDS + 1)
                for i in range(n):
                    last = products(masks[m][:, i, :], weights[:, t, :, :].rearrange("p k c -> p (k c)"),
                                    stop=(t == TILES - 1))
                    t += 1
                if t < TILES:
                    last.then_inc(s_used[m], 1)
            last.then_inc(s_acc, 1)


def kernel(r_x, L0_rec_emb_w, L0_rec_bias_w, L0_rec_g_bias):
    import numpy as np
    import concourse.bacc as bacc
    from concourse.bass_utils import run_bass_kernel_spmd

    x = np.asarray(r_x).reshape(P, GROUPS, FEATURES)
    arrays = {
        "x_t": np.ascontiguousarray(x.transpose(2, 1, 0)).reshape(FEATURES, BATCH),
        "emb": np.ascontiguousarray(L0_rec_emb_w),
        "bias": np.ascontiguousarray(L0_rec_bias_w),
        "g": np.ascontiguousarray(L0_rec_g_bias).reshape(1, 1),
    }
    nc = bacc.Bacc("TRN2", target_bir_lowering=False, num_devices=1)
    ins = [nc.dram_tensor(name, a.shape, mybir.dt.from_np(a.dtype), kind="ExternalInput").ap()
           for name, a in arrays.items()]
    out = nc.dram_tensor("y_out", (P, GROUPS), mybir.dt.float32, kind="ExternalOutput").ap()
    fm_kernel(nc, *ins, out)
    r = run_bass_kernel_spmd(nc, [arrays], core_ids=[0])
    return r.results[0]["y_out"].reshape(BATCH, 1)
```

```python
from contextlib import ExitStack

import concourse.bass as bass
from concourse import mybir

BATCH, FEATURES, DIM = 1024, 20000, 16
P = 128
TILES = FEATURES // P
REST = FEATURES - TILES * P
GROUPS = BATCH // P
COLS = DIM + 1
PARTS = 3

X_SLOTS = 6
MASK_SLOTS = 3
PIECE = 4
ROUNDS = 6
SLICES = [(0, 4), (4, 6), (6, 8)]
TAIL = [(n, 0, GROUPS) for n in (4, 4, 2, 1)] + [(1, g0, g1) for g0, g1 in SLICES]


def fm_kernel(nc, x_t, emb, bias, g, out):
    fp32, bf16, i32 = mybir.dt.float32, mybir.dt.bfloat16, mybir.dt.int32
    ALU = mybir.AluOpType
    AX_X = mybir.AxisListType.X

    assert ROUNDS * X_SLOTS * PIECE + sum(n * (g1 - g0) for n, g0, g1 in TAIL) // GROUPS == TILES
    assert X_SLOTS % MASK_SLOTS == 0 and len(SLICES) <= MASK_SLOTS
    USES = X_SLOTS // MASK_SLOTS

    x_main = x_t[0:TILES * P, :].rearrange("(p t) b -> p t b", t=TILES)
    x_rest = x_t[TILES * P:FEATURES, :]
    emb_main = emb[0:TILES * P, :].rearrange("(p t) d -> p t d", t=TILES)
    emb_rest = emb[TILES * P:FEATURES, :]
    bias_main = bias[0:TILES * P, :].rearrange("(p t) o -> p (t o)", t=TILES)
    bias_rest = bias[TILES * P:FEATURES, :]

    ctx = ExitStack()
    with ctx:
        def sb(name, shape, dt):
            return ctx.enter_context(nc.sbuf_tensor(name, shape, dt))

        def sem(name):
            return ctx.enter_context(nc.semaphore(name))

        tail, t0 = [], ROUNDS * X_SLOTS * PIECE
        for k, (n, g0, g1) in enumerate(TAIL, ROUNDS * X_SLOTS):
            tail.append((k, k % X_SLOTS, t0, n, g0, g1))
            t0 += n if g1 == GROUPS else 0

        x_ring = [sb(f"x_ring{s}", [P, PIECE, BATCH], i32) for s in range(X_SLOTS)]
        masks = [sb(f"masks{m}", [P, PIECE, BATCH], bf16) for m in range(MASK_SLOTS)]
        x_rem = sb("x_rem", [REST, BATCH], i32)
        mask_rem = sb("mask_rem", [REST + 1, BATCH], bf16)
        emb_raw = sb("emb_raw", [P, TILES + 1, DIM], fp32)
        emb_left = sb("emb_left", [P, TILES + 1, DIM], fp32)
        lin_raw = sb("lin_raw", [P, TILES + 1], fp32)
        emb_sq = sb("emb_sq", [P, TILES + 1], fp32)
        lin = sb("lin", [P, TILES + 1], fp32)
        lin_left = sb("lin_left", [P, TILES + 1], fp32)
        weights = sb("weights", [P, TILES + 1, PARTS, COLS], bf16)
        sums = sb("sums", [P, GROUPS, COLS], fp32)
        y = sb("y", [P, GROUPS], fp32)
        acc = ctx.enter_context(nc.psum_tensor("acc", [P, GROUPS, 512], fp32))

        s_blank = sem("s_blank")
        s_ones = sem("s_ones")
        s_w = sem("s_w")
        s_xrem = sem("s_xrem")
        s_prep = sem("s_prep")
        s_maskrem = sem("s_maskrem")
        s_x = [sem(f"s_x{s}") for s in range(X_SLOTS)]
        s_mask = [sem(f"s_mask{s}") for s in range(X_SLOTS)]
        s_used = [sem(f"s_used{m}") for m in range(MASK_SLOTS)]
        s_acc = sem("s_acc")
        s_fin = sem("s_fin")
        s_y = sem("s_y")
        s_out = sem("s_out")
        W_LOADS = 5

        block = ctx.enter_context(nc.Block())

        @block.sync
        def _(sp):
            sp.dma_start(emb_raw[:, 0:TILES, :], emb_main).then_inc(s_w, 16)
            sp.dma_start(lin_raw[:, 0:TILES], bias_main).then_inc(s_w, 16)
            sp.dma_start(x_rem[:, :], x_rest).then_inc(s_xrem, 16)
            for s in range(X_SLOTS):
                sp.dma_start(x_ring[s][:, :, :], x_main[:, s * PIECE:(s + 1) * PIECE, :]).then_inc(s_x[s], 16)
            with sp.Fori(1, ROUNDS) as r:
                for s in range(X_SLOTS):
                    sp.wait_ge(s_mask[s], r)
                    sp.dma_start(x_ring[s][:, :, :],
                                 x_main[:, bass.ds((r * X_SLOTS + s) * PIECE, PIECE), :]).then_inc(s_x[s], 16)
            for k, s, t, n, g0, g1 in tail:
                sp.wait_ge(s_mask[s], k // X_SLOTS)
                sp.dma_start(x_ring[s][:, 0:n, g0 * P:g1 * P],
                             x_main[:, t:t + n, g0 * P:g1 * P]).then_inc(s_x[s], 16)
            sp.wait_ge(s_y, 1)
            sp.dma_start(out, y[:, :]).then_inc(s_out, 16)
            sp.wait_ge(s_out, 16)

        @block.scalar
        def _(act):
            act.wait_ge(s_blank, 2)
            act.dma_start(emb_raw[0:REST, TILES, :], emb_rest).then_inc(s_w, 16)
            act.dma_start(lin_raw[0:REST, TILES:TILES + 1], bias_rest).then_inc(s_w, 16)
            act.dma_start(lin_raw[REST:REST + 1, TILES:TILES + 1], g).then_inc(s_w, 16)

        @block.gpsimd
        def _(pool):
            nc.gpsimd.memset(emb_raw[:, TILES, :], 0.0).then_inc(s_blank, 1)
            nc.gpsimd.memset(lin_raw[:, TILES:TILES + 1], 0.0).then_inc(s_blank, 1)
            pool.wait_ge(s_blank, 2)
            nc.gpsimd.memset(mask_rem[REST:REST + 1, :], 1.0).then_inc(s_ones, 1)

        @block.vector
        def _(dve):
            steps = [0]

            def done(ins):
                steps[0] += 1
                ins.then_inc(s_prep, 1)
                dve.wait_ge(s_prep, steps[0])

            dve.wait_ge(s_w, 16 * W_LOADS)
            done(nc.vector.tensor_tensor(emb_left[:, :, :], emb_raw[:, :, :], emb_raw[:, :, :], ALU.mult))
            done(nc.vector.tensor_reduce(emb_sq[:, :], emb_left[:, :, :], AX_X, ALU.add))
            done(nc.vector.scalar_tensor_tensor(lin[:, :], emb_sq[:, :], -0.5, lin_raw[:, :], ALU.mult, ALU.add))

            for whole, left, c0, c1 in ((emb_raw[:, :, :], emb_left[:, :, :], 0, DIM),
                                        (lin[:, :].unsqueeze(2), lin_left[:, :].unsqueeze(2), DIM, COLS)):
                high, mid, low = (weights[:, :, part, c0:c1] for part in range(PARTS))
                done(nc.vector.tensor_copy(high, whole))
                done(nc.vector.tensor_tensor(left, whole, high, ALU.subtract))
                done(nc.vector.tensor_copy(mid, left))
                done(nc.vector.tensor_tensor(low, left, mid, ALU.subtract))

            dve.wait_ge(s_xrem, 16)
            nc.vector.tensor_scalar(mask_rem[0:REST, :], x_rem[:, :], 0.0, None, ALU.is_gt).then_inc(s_maskrem, 1)
            for s in range(X_SLOTS):
                m = s % MASK_SLOTS
                dve.wait_ge(s_x[s], 16)
                if s >= MASK_SLOTS:
                    dve.wait_ge(s_used[m], s // MASK_SLOTS)
                nc.vector.tensor_scalar(masks[m][:, :, :], x_ring[s][:, :, :], 0.0, None,
                                        ALU.is_gt).then_inc(s_mask[s], 1)
            with dve.Fori(1, ROUNDS) as r:
                for s in range(X_SLOTS):
                    m = s % MASK_SLOTS
                    dve.wait_ge(s_x[s], (r + 1) * 16)
                    dve.wait_ge(s_used[m], r * USES + s // MASK_SLOTS)
                    nc.vector.tensor_scalar(masks[m][:, :, :], x_ring[s][:, :, :], 0.0, None,
                                            ALU.is_gt).then_inc(s_mask[s], 1)
            for k, s, t, n, g0, g1 in tail:
                m = k % MASK_SLOTS
                dve.wait_ge(s_x[s], (k // X_SLOTS + 1) * 16)
                dve.wait_ge(s_used[m], k // MASK_SLOTS)
                nc.vector.tensor_scalar(masks[m][:, 0:n, g0 * P:g1 * P], x_ring[s][:, 0:n, g0 * P:g1 * P],
                                        0.0, None, ALU.is_gt).then_inc(s_mask[s], 1)

            parts = acc[:, :, 0:PARTS * COLS].rearrange("p j (k c) -> p j c k", c=COLS)
            for n, (g0, g1) in enumerate(SLICES):
                dve.wait_ge(s_acc, n + 1)
                nc.vector.tensor_reduce(sums[:, g0:g1, :], parts[:, g0:g1, :, :], AX_X,
                                        ALU.add).then_inc(s_fin, 1)
            dve.wait_ge(s_fin, len(SLICES))
            ev = sums[:, :, 0:DIM]
            nc.vector.scalar_tensor_tensor(ev, ev, 0.5, ev, ALU.mult, ALU.mult).then_inc(s_fin, 1)
            dve.wait_ge(s_fin, len(SLICES) + 1)
            nc.vector.tensor_reduce(y[:, :], sums[:, :, :], AX_X, ALU.add).then_inc(s_y, 1)

        @block.tensor
        def _(pe):
            PREP_STEPS = 3 + 2 * 4

            def products(mask, w, g0=0, g1=GROUPS, start=False, stop=False):
                for j in range(g0, g1):
                    last = nc.tensor.matmul(acc[:, j, 0:PARTS * COLS], mask[:, j * P:(j + 1) * P], w,
                                            start=start, stop=stop)
                return last

            pe.wait_ge(s_prep, PREP_STEPS)
            pe.wait_ge(s_maskrem, 1)
            pe.wait_ge(s_ones, 1)
            products(mask_rem[:, :], weights[0:REST + 1, TILES, :, :].rearrange("p k c -> p (k c)"), start=True)
            with pe.Fori(0, ROUNDS) as r:
                for s in range(X_SLOTS):
                    m = s % MASK_SLOTS
                    pe.wait_ge(s_mask[s], r + 1)
                    for i in range(PIECE):
                        t = (r * X_SLOTS + s) * PIECE + i
                        w = weights[:, bass.ds(t, 1), :, :].rearrange("p t k c -> p (t k c)")
                        last = products(masks[m][:, i, :], w)
                    last.then_inc(s_used[m], 1)
            for k, s, t, n, g0, g1 in tail:
                m = k % MASK_SLOTS
                pe.wait_ge(s_mask[s], k // X_SLOTS + 1)
                for i in range(n):
                    last = products(masks[m][:, i, :], weights[:, t + i, :, :].rearrange("p k c -> p (k c)"),
                                    g0, g1, stop=(t + i == TILES - 1))
                last.then_inc(s_acc if t + n == TILES else s_used[m], 1)


def kernel(r_x, L0_rec_emb_w, L0_rec_bias_w, L0_rec_g_bias):
    import numpy as np
    import concourse.bacc as bacc
    from concourse.bass_utils import run_bass_kernel_spmd

    x = np.asarray(r_x).reshape(P, GROUPS, FEATURES)
    arrays = {
        "x_t": np.ascontiguousarray(x.transpose(2, 1, 0)).reshape(FEATURES, BATCH),
        "emb": np.ascontiguousarray(L0_rec_emb_w),
        "bias": np.ascontiguousarray(L0_rec_bias_w),
        "g": np.ascontiguousarray(L0_rec_g_bias).reshape(1, 1),
    }
    nc = bacc.Bacc("TRN2", target_bir_lowering=False, num_devices=1)
    ins = [nc.dram_tensor(name, a.shape, mybir.dt.from_np(a.dtype), kind="ExternalInput").ap()
           for name, a in arrays.items()]
    out = nc.dram_tensor("y_out", (P, GROUPS), mybir.dt.float32, kind="ExternalOutput").ap()
    fm_kernel(nc, *ins, out)
    r = run_bass_kernel_spmd(nc, [arrays], core_ids=[0])
    return r.results[0]["y_out"].reshape(BATCH, 1)
```
